# Optimizing a Trainium2 kernel written in Bass

```python
import numpy as np
import jax
import jax.numpy as jnp

def _softmax(x, axis=-1):
    return jax.nn.softmax(x, axis=axis)

def _gelu(x):
    return jax.nn.gelu(x, approximate=True)

def _silu(x):
    return jax.nn.silu(x)

def _sigmoid(x):
    return jax.nn.sigmoid(x)

def _layernorm(x, axis=-1, eps=1e-05):
    m = jnp.mean(x, axis=axis, keepdims=True)
    v = jnp.var(x, axis=axis, keepdims=True)
    return (x - m) / jnp.sqrt(v + eps)

def _scatter_add(tgt, idx, src, axis=0):
    return tgt.at[idx].add(src)

def _segment_sum(src, seg, n):
    return jax.ops.segment_sum(src, seg, n)
kernel_name = 'mk_dlrm_tower_d1_rec_r8_8aba16'

def setup_inputs(seed: int=0):
    np.random.seed(seed)
    _w = jnp.asarray

    def _rec_inputs():
        import jax
        import jax.numpy as jnp
        _tk = jax.random.key(seed)
        ids = jnp.stack([jax.random.randint(jax.random.fold_in(_tk, 200 + f), (512,), 0, v, jnp.int32) for f, v in enumerate([125000, 12500, 1250, 1000, 1000, 12500, 1250, 12500, 1250, 12500, 1250, 1000, 1000, 12500, 1250, 12500, 1000, 1000, 1250, 1000, 1000, 1250, 12500, 1000, 12500, 1000])], axis=1)
        tbl_0 = 0.05 * jax.random.normal(jax.random.fold_in(_tk, 500 + 0), (125000, 128), jnp.float32)
        tbl_1 = 0.05 * jax.random.normal(jax.random.fold_in(_tk, 500 + 1), (12500, 128), jnp.float32)
        tbl_2 = 0.05 * jax.random.normal(jax.random.fold_in(_tk, 500 + 2), (1250, 128), jnp.float32)
        tbl_3 = 0.05 * jax.random.normal(jax.random.fold_in(_tk, 500 + 3), (1000, 128), jnp.float32)
        tbl_4 = 0.05 * jax.random.normal(jax.random.fold_in(_tk, 500 + 4), (1000, 128), jnp.float32)
        tbl_5 = 0.05 * jax.random.normal(jax.random.fold_in(_tk, 500 + 5), (12500, 128), jnp.float32)
        tbl_6 = 0.05 * jax.random.normal(jax.random.fold_in(_tk, 500 + 6), (1250, 128), jnp.float32)
        tbl_7 = 0.05 * jax.random.normal(jax.random.fold_in(_tk, 500 + 7), (12500, 128), jnp.float32)
        tbl_8 = 0.05 * jax.random.normal(jax.random.fold_in(_tk, 500 + 8), (1250, 128), jnp.float32)
        tbl_9 = 0.05 * jax.random.normal(jax.random.fold_in(_tk, 500 + 9), (12500, 128), jnp.float32)
        tbl_10 = 0.05 * jax.random.normal(jax.random.fold_in(_tk, 500 + 10), (1250, 128), jnp.float32)
        tbl_11 = 0.05 * jax.random.normal(jax.random.fold_in(_tk, 500 + 11), (1000, 128), jnp.float32)
        tbl_12 = 0.05 * jax.random.normal(jax.random.fold_in(_tk, 500 + 12), (1000, 128), jnp.float32)
        tbl_13 = 0.05 * jax.random.normal(jax.random.fold_in(_tk, 500 + 13), (12500, 128), jnp.float32)
        tbl_14 = 0.05 * jax.random.normal(jax.random.fold_in(_tk, 500 + 14), (1250, 128), jnp.float32)
        tbl_15 = 0.05 * jax.random.normal(jax.random.fold_in(_tk, 500 + 15), (12500, 128), jnp.float32)
        tbl_16 = 0.05 * jax.random.normal(jax.random.fold_in(_tk, 500 + 16), (1000, 128), jnp.float32)
        tbl_17 = 0.05 * jax.random.normal(jax.random.fold_in(_tk, 500 + 17), (1000, 128), jnp.float32)
        tbl_18 = 0.05 * jax.random.normal(jax.random.fold_in(_tk, 500 + 18), (1250, 128), jnp.float32)
        tbl_19 = 0.05 * jax.random.normal(jax.random.fold_in(_tk, 500 + 19), (1000, 128), jnp.float32)
        tbl_20 = 0.05 * jax.random.normal(jax.random.fold_in(_tk, 500 + 20), (1000, 128), jnp.float32)
        tbl_21 = 0.05 * jax.random.normal(jax.random.fold_in(_tk, 500 + 21), (1250, 128), jnp.float32)
        tbl_22 = 0.05 * jax.random.normal(jax.random.fold_in(_tk, 500 + 22), (12500, 128), jnp.float32)
        tbl_23 = 0.05 * jax.random.normal(jax.random.fold_in(_tk, 500 + 23), (1000, 128), jnp.float32)
        tbl_24 = 0.05 * jax.random.normal(jax.random.fold_in(_tk, 500 + 24), (12500, 128), jnp.float32)
        tbl_25 = 0.05 * jax.random.normal(jax.random.fold_in(_tk, 500 + 25), (1000, 128), jnp.float32)
        _rk = jax.random.fold_in(_tk, 7)
        r_dense_features = -0.000520686 + 1.00062 * jax.random.normal(jax.random.fold_in(_rk, 101), (512, 128), jnp.float32)
        W_top1 = 0.0405887 * jax.random.normal(jax.random.fold_in(_tk, 801), (607, 512), jnp.float32)
        W_top2 = 0.0441942 * jax.random.normal(jax.random.fold_in(_tk, 802), (512, 256), jnp.float32)
        W_top3 = 0.0625 * jax.random.normal(jax.random.fold_in(_tk, 803), (256, 1), jnp.float32)
        b_top1 = jnp.zeros((512,), jnp.float32)
        b_top2 = jnp.zeros((256,), jnp.float32)
        return (r_dense_features, ids, tbl_0, tbl_1, tbl_2, tbl_3, tbl_4, tbl_5, tbl_6, tbl_7, tbl_8, tbl_9, tbl_10, tbl_11, tbl_12, tbl_13, tbl_14, tbl_15, tbl_16, tbl_17, tbl_18, tbl_19, tbl_20, tbl_21, tbl_22, tbl_23, tbl_24, tbl_25, W_top1, b_top1, W_top2, b_top2, W_top3)
    r_dense_features, ids, tbl_0, tbl_1, tbl_2, tbl_3, tbl_4, tbl_5, tbl_6, tbl_7, tbl_8, tbl_9, tbl_10, tbl_11, tbl_12, tbl_13, tbl_14, tbl_15, tbl_16, tbl_17, tbl_18, tbl_19, tbl_20, tbl_21, tbl_22, tbl_23, tbl_24, tbl_25, W_top1, b_top1, W_top2, b_top2, W_top3 = _rec_inputs()

    def _L0_rec_setup():
        import jax, jax.numpy as jnp
        import numpy as np
        F = 26
        B, D = (2048, 128)
        _IU0, _IU1 = np.triu_indices(F + 1, k=1)
        _IU0 = jnp.asarray(_IU0)
        _IU1 = jnp.asarray(_IU1)
        key = jax.random.key(seed)
        k1, k2 = jax.random.split(key)
        dense_features = jax.random.normal(k1, (B, D), dtype=jnp.float32)
        sparse_features = jax.random.normal(k2, (B, F, D), dtype=jnp.float32)
        return {'dense_features': dense_features, 'sparse_features': sparse_features}
    _L0_rec_all = _L0_rec_setup()
    _L0_rec_in = {k: v for k, v in _L0_rec_all.items() if k in ()}
    del _L0_rec_all
    return {'r_dense_features': r_dense_features, 'ids': ids, 'tbl_0': tbl_0, 'tbl_1': tbl_1, 'tbl_2': tbl_2, 'tbl_3': tbl_3, 'tbl_4': tbl_4, 'tbl_5': tbl_5, 'tbl_6': tbl_6, 'tbl_7': tbl_7, 'tbl_8': tbl_8, 'tbl_9': tbl_9, 'tbl_10': tbl_10, 'tbl_11': tbl_11, 'tbl_12': tbl_12, 'tbl_13': tbl_13, 'tbl_14': tbl_14, 'tbl_15': tbl_15, 'tbl_16': tbl_16, 'tbl_17': tbl_17, 'tbl_18': tbl_18, 'tbl_19': tbl_19, 'tbl_20': tbl_20, 'tbl_21': tbl_21, 'tbl_22': tbl_22, 'tbl_23': tbl_23, 'tbl_24': tbl_24, 'tbl_25': tbl_25, 'W_top1': W_top1, 'b_top1': b_top1, 'W_top2': W_top2, 'b_top2': b_top2, 'W_top3': W_top3}

def reference(r_dense_features, ids, tbl_0, tbl_1, tbl_2, tbl_3, tbl_4, tbl_5, tbl_6, tbl_7, tbl_8, tbl_9, tbl_10, tbl_11, tbl_12, tbl_13, tbl_14, tbl_15, tbl_16, tbl_17, tbl_18, tbl_19, tbl_20, tbl_21, tbl_22, tbl_23, tbl_24, tbl_25, W_top1, b_top1, W_top2, b_top2, W_top3):
    import jax
    import jax.numpy as jnp

    def _L0_rec_ref(dense_features, sparse_features):
        import jax, jax.numpy as jnp
        import numpy as np
        F = 26
        B, D = (2048, 128)
        _IU0, _IU1 = np.triu_indices(F + 1, k=1)
        _IU0 = jnp.asarray(_IU0)
        _IU1 = jnp.asarray(_IU1)
        combined = jnp.concatenate([dense_features[:, None, :], sparse_features], axis=1)
        interactions = jnp.einsum('bfd,bgd->bfg', combined, combined)
        interactions_flat = interactions[:, _IU0, _IU1]
        return jnp.concatenate([dense_features, interactions_flat], axis=1)
    e = jnp.stack([tbl_0[ids[:, 0]], tbl_1[ids[:, 1]], tbl_2[ids[:, 2]], tbl_3[ids[:, 3]], tbl_4[ids[:, 4]], tbl_5[ids[:, 5]], tbl_6[ids[:, 6]], tbl_7[ids[:, 7]], tbl_8[ids[:, 8]], tbl_9[ids[:, 9]], tbl_10[ids[:, 10]], tbl_11[ids[:, 11]], tbl_12[ids[:, 12]], tbl_13[ids[:, 13]], tbl_14[ids[:, 14]], tbl_15[ids[:, 15]], tbl_16[ids[:, 16]], tbl_17[ids[:, 17]], tbl_18[ids[:, 18]], tbl_19[ids[:, 19]], tbl_20[ids[:, 20]], tbl_21[ids[:, 21]], tbl_22[ids[:, 22]], tbl_23[ids[:, 23]], tbl_24[ids[:, 24]], tbl_25[ids[:, 25]]], axis=1)
    z = _L0_rec_ref(r_dense_features, e)
    z = z.reshape(z.shape[0], -1)
    h = jnp.concatenate([z, r_dense_features], axis=1)
    h = jnp.maximum(h @ W_top1 + b_top1, 0.0)
    h = jnp.maximum(h @ W_top2 + b_top2, 0.0)
    y = h @ W_top3
    return y

_drawn_inputs = setup_inputs


def setup_inputs(seed=0):
    import zlib

    import numpy as np

    out = dict(_drawn_inputs(seed))
    spreads = {'b_top1': (0.0, 0.1), 'b_top2': (0.0, 0.1)}
    factors = {}
    for name, (base, spread) in spreads.items():
        noise = np.random.default_rng([zlib.crc32(name.encode()), seed]).standard_normal(out[name].shape)
        drawn = base * np.exp(spread * noise) if base else spread * noise
        out[name] = jnp.asarray(drawn.astype(out[name].dtype))
    for name, factor in factors.items():
        out[name] = (out[name] * factor).astype(out[name].dtype)
    return out
```

```python
from contextlib import ExitStack

import concourse.bass as bass
from concourse import mybir
from concourse.alu_op_type import AluOpType as ALU

F32 = mybir.dt.float32
F32R = mybir.dt.float32r
I32 = mybir.dt.int32
ACT = mybir.ActivationFunctionType

P = 128
QUAD = 32
RING = 4


class Plan:

    LOOKED_UP = 8
    ROWS = 1000

    def __init__(self, table_rows):
        small = [f for f, rows in enumerate(table_rows) if rows == self.ROWS]
        self.by_product = small[:self.LOOKED_UP]
        self.gathered = [f for f in range(len(table_rows)) if f not in self.by_product]
        self.slots = [0] + [1 + f for f in self.gathered + self.by_product]
        self.n = len(self.slots)
        self.per_quad = -(-(self.n - 1) // 4)

    def pair_row(self, f, g):
        a, b = sorted((self.slots[f], self.slots[g]))
        return P + a * self.n - a * (a + 1) // 2 + (b - a - 1)


def build_tower(nc, plan, dense_t, gather_ids, product_ids, tables, w_pairs, W_top1, W_top2,
                b1_cols, b2_cols, w3_cols, out):
    D, B = dense_t.shape
    N1, N2 = W_top2.shape
    NT = B // P
    NG, NP = len(plan.gathered), len(plan.by_product)
    NV = plan.n
    J = plan.per_quad
    KR = next(k for k in range(P, 0, -1) if plan.ROWS % k == 0)
    KT = plan.ROWS // KR
    PER_BANK = 512 // P
    NB = -(-NG // PER_BANK)
    C1, C2 = N1 // P, N2 // P
    HALF = QUAD // 2
    assert D == P and NV <= QUAD and KT * KR == plan.ROWS and HALF * (NV - 1) <= 512 and C1 == 4

    turns = [[("turn", t, k) for k in range(NB)] for t in range(NT)]
    early = []
    waiting = list(turns[0])
    for n in range(NP):
        early.append(("lookup", n))
        if n >= 1 and waiting:
            early.append(waiting.pop(0))
    early += waiting

    def looked_up(n):
        return early.index(("lookup", n)) + 1

    with ExitStack() as ctx:
        def sb(name, shape, dt=F32):
            return ctx.enter_context(nc.sbuf_tensor(name, shape, dt))

        def ps(name, shape):
            return ctx.enter_context(nc.psum_tensor(name, shape, F32))

        def sem(name):
            return ctx.enter_context(nc.semaphore(name))

        ids_g = sb("ids_g", [P, NT * NG], I32)
        ids_p = sb("ids_p", [KR, RING, B], I32)
        raw = sb("raw", [KR, RING, KT * D])
        high = sb("high", [KR, 2, KT * D], F32R)
        low = sb("low", [KR, 2, KT * D], F32R)
        onehot = sb("onehot", [KR, 2 * KT, B], F32R)
        row_int = sb("row_int", [P, KT], I32)
        row_no = sb("row_no", [P, KT])
        ident = sb("ident", [P, P])
        rows = sb("rows", [P, NT, NG, D])
        dense = sb("dense", [D, B])
        vecs = sb("vecs", [D, B, NV])
        pairs = sb("pairs", [P, 2, J, P])
        wp = sb("wp", [P, J, N1])
        wd_ab = sb("wd_ab", [D, 2, N1])
        wd = sb("wd", [D, N1])
        w2 = sb("w2", [P, C1, N2])
        w3 = sb("w3", [P, C2])
        b1 = sb("b1", [P, C1])
        b2 = sb("b2", [P, C2])
        h1 = sb("h1", [P, 2, C1, P])
        h2 = sb("h2", [P, 2, C2, P])
        y = sb("y", [1, B])

        bank = [ps(f"bank{k}", [P, 512]) for k in range(2)]
        gram = [ps(f"gram{k}", [P, 2, 512]) for k in range(2)]
        topA = ps("topA", [P, 512])
        topB = ps("topB", [P, 512])

        ids_g_in = sem("ids_g_in")
        table_in = [sem(f"table_in{n}") for n in range(NP)]
        dense_in = sem("dense_in")
        wp_in = sem("wp_in")
        wd_in = sem("wd_in")
        small_in = sem("small_in")
        rows_in = [[sem(f"rows_in{t}_{k}") for k in range(NB)] for t in range(NT)]
        out_done = sem("out_done")
        ident_zeroed = sem("ident_zeroed")
        pairs_zeroed = sem("pairs_zeroed")
        ident_ready = sem("ident_ready")
        iota_done = sem("iota_done")
        row_no_ready = sem("row_no_ready")
        high_ready = sem("high_ready")
        low_ready = sem("low_ready")
        onehot_ready = sem("onehot_ready")
        bank_full = sem("bank_full")
        bank_copied = sem("bank_copied")
        dense_ready = sem("dense_ready")
        gram_ready = sem("gram_ready")
        pairs_act = sem("pairs_act")
        pairs_dve = sem("pairs_dve")
        l1a = sem("l1a")
        l1b = sem("l1b")
        h1a_ready = sem("h1a_ready")
        h1b_ready = sem("h1b_ready")
        l2_done = sem("l2_done")
        h2_ready = sem("h2_ready")
        l3_done = sem("l3_done")
        y_ready = sem("y_ready")

        block = ctx.enter_context(nc.Block())

        def spread(copy, t, i):
            for q in range(4):
                n = min(J, NV - 1 - J * q)
                src = gram[t % 2][QUAD * i:QUAD * i + NV, :, 0:HALF * (NV - 1)].rearrange(
                    "f k (c g) -> f k c g", g=NV - 1)[:, :, :, J * q:J * q + n]
                dst = pairs[QUAD * q:QUAD * q + NV, t % 2, 0:n, QUAD * i:QUAD * (i + 1)].rearrange(
                    "f j (k c) -> f k c j", k=2)
                last = copy(dst, src)
            return last

        @block.sync
        def _(sp):
            sp.dma_start(ids_g[:, :], gather_ids).then_inc(ids_g_in, 16)

            def table(n):
                if n >= RING:
                    sp.wait_ge(low_ready, n - RING + 1)
                    sp.wait_ge(onehot_ready, (n - RING + 1) * KT)
                sp.dma_start(raw[:, n % RING, :], tables[plan.by_product[n]].rearrange(
                    "(p k) d -> p (k d)", k=KT)).then_inc(table_in[n], 16)
                sp.dma_start(ids_p[:, n % RING, :], product_ids[n:n + 1, :].to_broadcast([KR, B])).then_inc(table_in[n], 16)

            def load_weights():
                sp.dma_start(wp[:, :, :], w_pairs).then_inc(wp_in, 16)
                sp.dma_start(w2[:, :, :], W_top2.rearrange("(c p) n -> p c n", p=P)).then_inc(small_in, 16)
                sp.dma_start(w3[:, :], w3_cols).then_inc(small_in, 16)
                sp.dma_start(b1[:, :], b1_cols).then_inc(small_in, 16)
                sp.dma_start(b2[:, :], b2_cols).then_inc(small_in, 16)

            table(0)
            table(1)
            sp.dma_start(dense[:, :], dense_t).then_inc(dense_in, 16)
            sp.dma_start(wd_ab[:, 0, :], W_top1[0:D, :]).then_inc(wd_in, 16)
            sp.dma_start(wd_ab[:, 1, :], W_top1[W_top1.shape[0] - D:, :]).then_inc(wd_in, 16)
            for n in range(2, NP):
                table(n)
                if n == RING - 1:
                    load_weights()
            sp.wait_ge(y_ready, NT)
            sp.dma_start(out, y[:, :]).then_inc(out_done, 16)
            sp.wait_ge(out_done, 16)

        @block.gpsimd
        def _(pool):
            pool.iota(row_int[:, :], pattern=[[1, KT]], base=0, channel_multiplier=KT).then_inc(iota_done, 1)
            pool.memset(ident[:, :], 0.0).then_inc(ident_zeroed, 1)
            pool.wait_ge(ident_zeroed, 1)
            pool.affine_select(out=ident[:, :], in_=ident[:, :], compare_op=ALU.not_equal, fill=1.0, base=0,
                               pattern=[[-1, P]], channel_multiplier=1).then_inc(ident_ready, 1)
            pool.wait_ge(ids_g_in, 16)
            for t in range(NT):
                for s, f in enumerate(plan.gathered):
                    pool.indirect_dma_start(
                        rows[:, t, s, :], None, tables[f],
                        bass.IndirectOffsetOnAxis(ap=ids_g[:, t * NG + s:t * NG + s + 1], axis=0),
                    ).then_inc(rows_in[t][s // PER_BANK], 16)

        @block.scalar
        def _(act):
            def split_high(n):
                act.wait_ge(table_in[n], 32)
                if n >= 2:
                    act.wait_ge(bank_full, looked_up(n - 2))
                act.activation(high[:, n % 2, :], raw[:, n % RING, :], ACT.Copy).then_inc(high_ready, 1)

            copied = [0]

            def copy_bank(item):
                m = copied[0]
                copied[0] += 1
                act.wait_ge(bank_full, m + 1)
                if item[0] == "lookup":
                    dst, src = vecs[:, :, 1 + NG + item[1]], bank[m % 2][:, :]
                else:
                    _, t, k = item
                    s = PER_BANK * k
                    n = min(PER_BANK, NG - s)
                    dst = vecs[:, t * P:(t + 1) * P, 1 + s:1 + s + n].rearrange("d b s -> d s b")
                    src = bank[m % 2][:, 0:n * P].rearrange("d (s b) -> d s b", s=n)
                act.activation(dst, src, ACT.Copy).then_inc(bank_copied, 1)

            def spread_act(t):
                act.wait_ge(gram_ready, t + 1)
                if t == 0:
                    act.wait_ge(pairs_zeroed, 1)
                if t >= 2:
                    act.wait_ge(l1b, t - 1)
                for i in (0, 1):
                    spread(lambda o, x: act.activation(o, x, ACT.Copy), t, i).then_inc(pairs_act, 1)

            def relu1(t):
                if t == 0:
                    act.wait_ge(small_in, 64)
                act.wait_ge(l1a, t + 1)
                if t >= 2:
                    act.wait_ge(l2_done, t - 1)
                for c in (0, 1):
                    act.activation(h1[:, t % 2, c, :], topA[:, c * P:(c + 1) * P], ACT.Relu,
                                   bias=b1[:, c:c + 1]).then_inc(h1a_ready, 1)

            def relu2(t):
                act.wait_ge(l2_done, t + 1)
                if t >= 2:
                    act.wait_ge(l3_done, t - 1)
                for c in range(C2):
                    act.activation(h2[:, t % 2, c, :], topA[:, 256 + c * P:256 + (c + 1) * P], ACT.Relu,
                                   bias=b2[:, c:c + 1]).then_inc(h2_ready, 1)

            split_high(0)
            split_high(1)
            for item in early:
                copy_bank(item)
                if item[0] == "lookup" and item[1] + 2 < NP:
                    split_high(item[1] + 2)
            for t in range(NT):
                spread_act(t)
                if t >= 1:
                    relu2(t - 1)
                if t + 1 < NT:
                    for item in turns[t + 1][:2]:
                        copy_bank(item)
                relu1(t)
                if t + 1 < NT:
                    for item in turns[t + 1][2:]:
                        copy_bank(item)
            relu2(NT - 1)

        @block.vector
        def _(dve):
            dve.memset(pairs[:, :, :, :], 0.0).then_inc(pairs_zeroed, 1)
            dve.wait_ge(iota_done, 1)
            dve.tensor_copy(row_no[:, :], row_int[:, :]).then_inc(row_no_ready, 1)
            dve.wait_ge(row_no_ready, 1)

            def compare(n, k):
                dve.tensor_scalar(onehot[:, (n % 2) * KT + k, :], ids_p[:, n % RING, :], row_no[0:KR, k:k + 1], None,
                                  ALU.is_equal).then_inc(onehot_ready, 1)

            for n in range(NP):
                dve.wait_ge(table_in[n], 32)
                if n >= 2:
                    dve.wait_ge(bank_full, looked_up(n - 2))
                compare(n, 0)
                dve.wait_ge(high_ready, n + 1)
                dve.tensor_tensor(low[:, n % 2, :], raw[:, n % RING, :], high[:, n % 2, :].bitcast(F32),
                                  ALU.subtract).then_inc(low_ready, 1)
                for k in range(1, KT):
                    compare(n, k)
                if n == 1:
                    dve.wait_ge(dense_in, 16)
                    dve.tensor_copy(vecs[:, :, 0], dense[:, :]).then_inc(dense_ready, 1)
                    dve.wait_ge(wd_in, 32)
                    dve.tensor_tensor(wd[:, :], wd_ab[:, 0, :], wd_ab[:, 1, :], ALU.add).then_inc(dense_ready, 1)

            def spread_dve(t):
                dve.wait_ge(gram_ready, t + 1)
                if t == 0:
                    dve.wait_ge(pairs_zeroed, 1)
                if t >= 2:
                    dve.wait_ge(l1b, t - 1)
                for i in (2, 3):
                    spread(lambda o, x: dve.tensor_copy(o, x), t, i).then_inc(pairs_dve, 1)

            def relu1(t):
                if t == 0:
                    dve.wait_ge(small_in, 64)
                dve.wait_ge(l1b, t + 1)
                if t >= 2:
                    dve.wait_ge(l2_done, t - 1)
                for c in (2, 3):
                    dve.tensor_scalar(h1[:, t % 2, c, :], topB[:, (c - 2) * P:(c - 1) * P], b1[:, c:c + 1], 0.0,
                                      ALU.add, ALU.max).then_inc(h1b_ready, 1)

            def copy_y(t):
                dve.wait_ge(l3_done, t + 1)
                dve.tensor_copy(y[0:1, t * P:(t + 1) * P], topB[0:1, 256:256 + P]).then_inc(y_ready, 1)

            for t in range(NT):
                spread_dve(t)
                if t >= 1:
                    copy_y(t - 1)
                relu1(t)
            copy_y(NT - 1)

        @block.tensor
        def _(pe):
            filled = [0]

            def fill_bank(item):
                m = filled[0]
                filled[0] += 1
                if m >= 2:
                    pe.wait_ge(bank_copied, m - 1)
                dst = bank[m % 2]
                if item[0] == "lookup":
                    n = item[1]
                    for k in range(KT):
                        pe.wait_ge(onehot_ready, n * KT + k + 1)
                        if k == 0:
                            pe.wait_ge(high_ready, n + 1)
                        hot = onehot[:, (n % 2) * KT + k, :]
                        pe.matmul(dst[:, :], high[:, n % 2, k * D:(k + 1) * D], hot, start=(k == 0), stop=False)
                        if k == 0:
                            pe.wait_ge(low_ready, n + 1)
                        last = pe.matmul(dst[:, :], low[:, n % 2, k * D:(k + 1) * D], hot, start=False,
                                         stop=(k == KT - 1))
                    last.then_inc(bank_full, 1)
                else:
                    _, t, k = item
                    s, n = PER_BANK * k, min(PER_BANK, NG - PER_BANK * k)
                    pe.wait_ge(rows_in[t][k], 16 * n)
                    for x in range(n):
                        last = pe.transpose(dst[:, x * P:(x + 1) * P], rows[:, t, s + x, :], ident[:, :])
                    last.then_inc(bank_full, 1)

            def make_gram(t, copied):
                pe.wait_ge(bank_copied, copied)
                if t == 0:
                    pe.wait_ge(dense_ready, 2)
                if t >= 2:
                    pe.wait_ge(pairs_act, 2 * (t - 1))
                    pe.wait_ge(pairs_dve, 2 * (t - 1))
                for c in range(QUAD):
                    for i in range(4):
                        b = t * P + QUAD * i + c
                        col = (c % HALF) * (NV - 1)
                        last = pe.matmul(gram[t % 2][QUAD * i:QUAD * i + NV, c // HALF, col:col + NV - 1],
                                         vecs[:, b, 0:NV], vecs[:, b, 1:NV], start=True, stop=True)
                last.then_inc(gram_ready, 1)

            def layer1(t):
                if t == 0:
                    pe.wait_ge(wp_in, 16)
                pe.wait_ge(pairs_act, 2 * (t + 1))
                pe.wait_ge(pairs_dve, 2 * (t + 1))
                if t >= 1:
                    pe.wait_ge(h2_ready, C2 * t)
                for c in range(C1):
                    if t >= 1 and c == 2:
                        pe.wait_ge(y_ready, t)
                    dst = (topA, topB)[c // 2][:, (c % 2) * P:(c % 2 + 1) * P]
                    n = slice(c * P, (c + 1) * P)
                    pe.matmul(dst, wd[:, n], dense[:, t * P:(t + 1) * P], start=True, stop=False)
                    for j in range(J):
                        last = pe.matmul(dst, wp[:, j, n], pairs[:, t % 2, j, :], start=False, stop=(j == J - 1))
                    if c == 1:
                        last.then_inc(l1a, 1)
                last.then_inc(l1b, 1)

            def layer2(t):
                pe.wait_ge(h1a_ready, 2 * (t + 1))
                pe.wait_ge(h1b_ready, 2 * (t + 1))
                for c2 in range(C2):
                    dst = topA[:, 256 + c2 * P:256 + (c2 + 1) * P]
                    for c in range(C1):
                        last = pe.matmul(dst, w2[:, c, c2 * P:(c2 + 1) * P], h1[:, t % 2, c, :], start=(c == 0),
                                         stop=(c == C1 - 1))
                last.then_inc(l2_done, 1)

            def layer3(t):
                pe.wait_ge(h2_ready, C2 * (t + 1))
                for c in range(C2):
                    last = pe.matmul(topB[0:1, 256:256 + P], w3[:, c:c + 1], h2[:, t % 2, c, :], start=(c == 0),
                                     stop=(c == C2 - 1))
                last.then_inc(l3_done, 1)

            pe.wait_ge(ident_ready, 1)
            for item in early:
                fill_bank(item)
            done = len(early)
            for t in range(NT):
                make_gram(t, done)
                if t == 0:
                    pe.wait_ge(small_in, 64)
                if t >= 1:
                    layer2(t - 1)
                if t + 1 < NT:
                    for item in turns[t + 1][:2]:
                        fill_bank(item)
                if t >= 1:
                    layer3(t - 1)
                layer1(t)
                if t + 1 < NT:
                    for item in turns[t + 1][2:]:
                        fill_bank(item)
                    done += NB
            layer2(NT - 1)
            layer3(NT - 1)


def kernel(**inputs):
    import numpy as np
    import concourse.bacc as bacc
    from concourse.bass_utils import run_bass_kernel_spmd

    dense = np.asarray(inputs["r_dense_features"])
    ids = np.asarray(inputs["ids"])
    B, F = ids.shape
    tables = [np.ascontiguousarray(inputs[f"tbl_{f}"]) for f in range(F)]
    plan = Plan([t.shape[0] for t in tables])
    W_top1 = np.ascontiguousarray(inputs["W_top1"])
    C1, C2 = inputs["b_top1"].shape[0] // P, inputs["b_top2"].shape[0] // P

    w_pairs = np.zeros((P, plan.per_quad, W_top1.shape[1]), W_top1.dtype)
    for g in range(1, plan.n):
        q, j = divmod(g - 1, plan.per_quad)
        for f in range(g):
            w_pairs[QUAD * q + f, j] = W_top1[plan.pair_row(f, g)]

    by_tile = ids.reshape(B // P, P, F).transpose(1, 0, 2)
    arrays = {
        "dense_t": np.ascontiguousarray(dense.T),
        "gather_ids": np.ascontiguousarray(by_tile[:, :, plan.gathered]).reshape(P, -1),
        "product_ids": np.ascontiguousarray(ids.T[plan.by_product]),
        "w_pairs": w_pairs,
        "W_top1": W_top1,
        "W_top2": np.ascontiguousarray(inputs["W_top2"]),
        "b1_cols": np.ascontiguousarray(np.asarray(inputs["b_top1"]).reshape(C1, P).T),
        "b2_cols": np.ascontiguousarray(np.asarray(inputs["b_top2"]).reshape(C2, P).T),
        "w3_cols": np.ascontiguousarray(np.asarray(inputs["W_top3"]).reshape(C2, P).T),
    }
    arrays |= {f"tbl_{f}": t for f, t in enumerate(tables)}

    nc = bacc.Bacc("TRN2", target_bir_lowering=False, num_devices=1)
    ap = {n: nc.dram_tensor(n, a.shape, mybir.dt.from_np(a.dtype), kind="ExternalInput").ap()
          for n, a in arrays.items()}
    y = nc.dram_tensor("y_out", (B, 1), F32, kind="ExternalOutput").ap()
    build_tower(nc, plan, ap["dense_t"], ap["gather_ids"], ap["product_ids"],
                [ap[f"tbl_{f}"] for f in range(F)], ap["w_pairs"], ap["W_top1"], ap["W_top2"],
                ap["b1_cols"], ap["b2_cols"], ap["w3_cols"], y.rearrange("b o -> o b"))
    r = run_bass_kernel_spmd(nc, [arrays], core_ids=[0])
    return r.results[0]["y_out"]
```

```python
from contextlib import ExitStack

import concourse.bass as bass
from concourse import mybir
from concourse.alu_op_type import AluOpType as ALU

F32 = mybir.dt.float32
F32R = mybir.dt.float32r
I32 = mybir.dt.int32
ACT = mybir.ActivationFunctionType

P = 128
QUAD = 32
RING = 3
ACT_TILES = 1


class Plan:

    LOOKED_UP = 8
    ROWS = 1000

    def __init__(self, table_rows):
        small = [f for f, rows in enumerate(table_rows) if rows == self.ROWS]
        self.by_product = small[:self.LOOKED_UP]
        self.gathered = [f for f in range(len(table_rows)) if f not in self.by_product]
        self.slots = [0] + [1 + f for f in self.gathered + self.by_product]
        self.n = len(self.slots)
        self.steps = (self.n - 1) // 2
        assert self.n % 2 == 1
        self.per_block = next(f for f in range(self.n, 0, -1) if self.n % f == 0 and f * self.steps <= P)
        self.blocks = self.n // self.per_block

    def pair_row(self, f, g):
        a, b = sorted((self.slots[f], self.slots[g]))
        return P + a * self.n - a * (a + 1) // 2 + (b - a - 1)


def build_tower(nc, plan, dense_t, gather_ids, product_ids, tables, w_pairs, W_top1, W_top2,
                b1_cols, b2_cols, w3_cols, out):
    D, B = dense_t.shape
    N1, N2 = W_top2.shape
    NT = B // P
    NG, NP = len(plan.gathered), len(plan.by_product)
    NV = plan.n
    K, FB, NBLK = plan.steps, plan.per_block, plan.blocks
    PB = FB * K
    KR = next(k for k in range(P, 0, -1) if plan.ROWS % k == 0)
    KT = plan.ROWS // KR
    KV = KT - ACT_TILES
    PER_BANK = 512 // P
    NB = -(-NG // PER_BANK)
    C1, C2 = N1 // P, N2 // P
    HALF = QUAD // 2
    assert D == P and NV <= QUAD and KT * KR == plan.ROWS and HALF * NV <= 512 and C1 == 4

    turns = [[("turn", t, k) for k in range(NB)] for t in range(NT)]

    def next_turns(t):
        return turns[t + 1] if t + 1 < NT else []

    early = []
    waiting = list(turns[0])
    for n in range(NP):
        early.append(("lookup", n))
        if n >= 1 and waiting:
            early.append(waiting.pop(0))
    early += waiting
    order = list(early)
    for t in range(NT):
        order += next_turns(t)[:2] + [("pairs", t)] + next_turns(t)[2:]

    def looked_up(n):
        return order.index(("lookup", n)) + 1

    def vectors(t):
        return max(order.index(("turn", t, NB - 1)), order.index(("lookup", NP - 1))) + 1

    def paired(t):
        return order.index(("pairs", t)) + 1

    with ExitStack() as ctx:
        def sb(name, shape, dt=F32):
            return ctx.enter_context(nc.sbuf_tensor(name, shape, dt))

        def ps(name, shape):
            return ctx.enter_context(nc.psum_tensor(name, shape, F32))

        def sem(name):
            return ctx.enter_context(nc.semaphore(name))

        ids_g = sb("ids_g", [P, NT * NG], I32)
        ids_p = sb("ids_p", [KR, RING, B], I32)
        raw = sb("raw", [KR, RING, KT * D])
        high = sb("high", [KR, 2, KT * D], F32R)
        low = sb("low", [KR, 2, KT * D], F32R)
        onehot = sb("onehot", [KR, 2 * KT, B], F32R)
        row_int = sb("row_int", [P, KT], I32)
        row_no = sb("row_no", [P, KT])
        minus_row_no = sb("minus_row_no", [P, KT])
        distance = sb("distance", [KR, 2, B])
        ident = sb("ident", [P, P])
        rows = sb("rows", [P, NT, NG, D])
        dense = sb("dense", [D, B])
        vecs = sb("vecs", [D, B, NV])
        grid = sb("grid", [P, 2, NV + K, QUAD])
        packed = sb("packed", [P, 2, NBLK * PB])
        pairs = sb("pairs", [PB, 2, NBLK, P])
        wp = sb("wp", [PB, NBLK, N1])
        wd_ab = sb("wd_ab", [D, 2, N1])
        wd = sb("wd", [D, N1])
        w2 = sb("w2", [P, C1, N2])
        w3 = sb("w3", [P, C2])
        b1 = sb("b1", [P, C1])
        b2 = sb("b2", [P, C2])
        h1 = sb("h1", [P, 2, C1, P])
        h2 = sb("h2", [P, 2, C2, P])
        y = sb("y", [1, B])

        bank = [ps(f"bank{k}", [P, 512]) for k in range(2)]
        gram = [ps(f"gram{k}", [P, 2, 512]) for k in range(2)]
        topA = ps("topA", [P, 512])
        topB = ps("topB", [P, 512])

        ids_g_in = sem("ids_g_in")
        table_in = [sem(f"table_in{n}") for n in range(NP)]
        dense_in = sem("dense_in")
        wp_in = sem("wp_in")
        wd_in = sem("wd_in")
        small_in = sem("small_in")
        rows_in = [[sem(f"rows_in{t}_{k}") for k in range(NB)] for t in range(NT)]
        out_done = sem("out_done")
        ident_zeroed = sem("ident_zeroed")
        gram_zeroed = sem("gram_zeroed")
        ident_ready = sem("ident_ready")
        iota_done = sem("iota_done")
        row_no_ready = sem("row_no_ready")
        high_ready = sem("high_ready")
        low_ready = sem("low_ready")
        onehot_dve = sem("onehot_dve")
        onehot_act = sem("onehot_act")
        distance_ready = sem("distance_ready")
        bank_full = sem("bank_full")
        bank_copied = sem("bank_copied")
        dense_ready = sem("dense_ready")
        gram_ready = sem("gram_ready")
        grid_turned = sem("grid_turned")
        grid_ready = sem("grid_ready")
        packed_ready = sem("packed_ready")
        l1a = sem("l1a")
        l1b = sem("l1b")
        h1a_ready = sem("h1a_ready")
        h1b_ready = sem("h1b_ready")
        l2_done = sem("l2_done")
        h2_ready = sem("h2_ready")
        l3_done = sem("l3_done")
        y_ready = sem("y_ready")

        block = ctx.enter_context(nc.Block())

        @block.sync
        def _(sp):
            def table(n):
                if n >= RING:
                    sp.wait_ge(low_ready, n - RING + 1)
                    sp.wait_ge(onehot_dve, (n - RING + 1) * KV)
                    sp.wait_ge(onehot_act, (n - RING + 1) * ACT_TILES)
                sp.dma_start(raw[:, n % RING, :], tables[plan.by_product[n]].rearrange(
                    "(p k) d -> p (k d)", k=KT)).then_inc(table_in[n], 16)
                sp.dma_start(ids_p[:, n % RING, :], product_ids[n:n + 1, :].to_broadcast([KR, B])).then_inc(table_in[n], 16)

            def load_weights():
                sp.dma_start(wp[:, :, :], w_pairs).then_inc(wp_in, 16)
                sp.dma_start(w2[:, :, :], W_top2.rearrange("(c p) n -> p c n", p=P)).then_inc(small_in, 16)
                sp.dma_start(w3[:, :], w3_cols).then_inc(small_in, 16)
                sp.dma_start(b1[:, :], b1_cols).then_inc(small_in, 16)
                sp.dma_start(b2[:, :], b2_cols).then_inc(small_in, 16)

            for n in range(NP):
                table(n)
            sp.dma_start(dense[:, :], dense_t).then_inc(dense_in, 16)
            sp.dma_start(wd_ab[:, 0, :], W_top1[0:D, :]).then_inc(wd_in, 16)
            sp.dma_start(wd_ab[:, 1, :], W_top1[W_top1.shape[0] - D:, :]).then_inc(wd_in, 16)
            load_weights()
            sp.wait_ge(y_ready, NT)
            sp.dma_start(out, y[:, :]).then_inc(out_done, 16)
            sp.wait_ge(out_done, 16)

        @block.gpsimd
        def _(pool):
            pool.iota(row_int[:, :], pattern=[[1, KT]], base=0, channel_multiplier=KT).then_inc(iota_done, 1)
            pool.memset(ident[:, :], 0.0).then_inc(ident_zeroed, 1)
            pool.wait_ge(ident_zeroed, 1)
            pool.affine_select(out=ident[:, :], in_=ident[:, :], compare_op=ALU.not_equal, fill=1.0, base=0,
                               pattern=[[-1, P]], channel_multiplier=1).then_inc(ident_ready, 1)
            pool.wait_ge(ids_g_in, 16)
            for t in range(NT):
                for s, f in enumerate(plan.gathered):
                    pool.indirect_dma_start(
                        rows[:, t, s, :], None, tables[f],
                        bass.IndirectOffsetOnAxis(ap=ids_g[:, t * NG + s:t * NG + s + 1], axis=0),
                    ).then_inc(rows_in[t][s // PER_BANK], 16)

        @block.scalar
        def _(act):
            def split_high(n):
                act.wait_ge(table_in[n], 32)
                if n >= 2:
                    act.wait_ge(bank_full, looked_up(n - 2))
                act.activation(high[:, n % 2, :], raw[:, n % RING, :], ACT.Copy).then_inc(high_ready, 1)

            def compare(n):
                for x in range(ACT_TILES):
                    made = n * ACT_TILES + x
                    k = KV + x
                    act.activation(distance[:, made % 2, :], ids_p[:, n % RING, :], ACT.Abs,
                                   bias=minus_row_no[0:KR, k:k + 1]).then_inc(distance_ready, 1)
                    act.wait_ge(distance_ready, made + 1)
                    act.activation(onehot[:, (n % 2) * KT + k, :], distance[:, made % 2, :], ACT.Relu,
                                   bias=1.0, scale=-1.0).then_inc(onehot_act, 1)

            copied = [0]

            def copy_bank(item):
                m = copied[0]
                copied[0] += 1
                act.wait_ge(bank_full, m + 1)
                if item[0] == "lookup":
                    dst, src = vecs[:, :, 1 + NG + item[1]], bank[m % 2][:, :]
                elif item[0] == "pairs":
                    t = item[1]
                    if t >= 2:
                        act.wait_ge(l1b, t - 1)
                    dst = pairs[:, t % 2, :, :]
                    src = bank[m % 2][0:PB, 0:NBLK * P].rearrange("p (k b) -> p k b", k=NBLK)
                else:
                    _, t, k = item
                    s = PER_BANK * k
                    n = min(PER_BANK, NG - s)
                    dst = vecs[:, t * P:(t + 1) * P, 1 + s:1 + s + n].rearrange("d b s -> d s b")
                    src = bank[m % 2][:, 0:n * P].rearrange("d (s b) -> d s b", s=n)
                act.activation(dst, src, ACT.Copy).then_inc(bank_copied, 1)

            def relu1(t):
                if t == 0:
                    act.wait_ge(small_in, 64)
                act.wait_ge(l1a, t + 1)
                if t >= 2:
                    act.wait_ge(l2_done, t - 1)
                for c in (0, 1):
                    act.activation(h1[:, t % 2, c, :], topA[:, c * P:(c + 1) * P], ACT.Relu,
                                   bias=b1[:, c:c + 1]).then_inc(h1a_ready, 1)

            def relu2(t):
                act.wait_ge(l2_done, t + 1)
                if t >= 2:
                    act.wait_ge(l3_done, t - 1)
                for c in range(C2):
                    act.activation(h2[:, t % 2, c, :], topA[:, 256 + c * P:256 + (c + 1) * P], ACT.Relu,
                                   bias=b2[:, c:c + 1]).then_inc(h2_ready, 1)

            act.dma_start(ids_g[:, :], gather_ids).then_inc(ids_g_in, 16)
            split_high(0)
            act.wait_ge(row_no_ready, 2)
            compare(0)
            split_high(1)
            compare(1)
            for item in early:
                copy_bank(item)
                if item[0] == "lookup" and item[1] + 2 < NP:
                    split_high(item[1] + 2)
                    compare(item[1] + 2)
            for t in range(NT):
                for item in next_turns(t)[:2] + [("pairs", t)] + next_turns(t)[2:3]:
                    copy_bank(item)
                relu1(t)
                for item in next_turns(t)[3:]:
                    copy_bank(item)
                relu2(t)

        @block.vector
        def _(dve):
            for k in range(2):
                dve.memset(gram[k][:, :, :], 0.0).then_inc(gram_zeroed, 1)
            dve.wait_ge(iota_done, 1)
            dve.tensor_copy(row_no[:, :], row_int[:, :]).then_inc(row_no_ready, 1)
            dve.wait_ge(row_no_ready, 1)
            dve.tensor_scalar(minus_row_no[:, :], row_no[:, :], -1.0, None, ALU.mult).then_inc(row_no_ready, 1)

            def compare(n, k):
                dve.tensor_scalar(onehot[:, (n % 2) * KT + k, :], ids_p[:, n % RING, :], row_no[0:KR, k:k + 1], None,
                                  ALU.is_equal).then_inc(onehot_dve, 1)

            for n in range(NP):
                dve.wait_ge(table_in[n], 32)
                if n >= 2:
                    dve.wait_ge(bank_full, looked_up(n - 2))
                compare(n, 0)
                dve.wait_ge(high_ready, n + 1)
                dve.tensor_tensor(low[:, n % 2, :], raw[:, n % RING, :], high[:, n % 2, :].bitcast(F32),
                                  ALU.subtract).then_inc(low_ready, 1)
                for k in range(1, KV):
                    compare(n, k)
            dve.wait_ge(dense_in, 16)
            dve.tensor_copy(vecs[:, :, 0], dense[:, :]).then_inc(dense_ready, 1)
            dve.wait_ge(wd_in, 32)
            dve.tensor_tensor(wd[:, :], wd_ab[:, 0, :], wd_ab[:, 1, :], ALU.add).then_inc(dense_ready, 1)

            def make_grid(t):
                dve.wait_ge(gram_ready, t + 1)
                if t >= 2:
                    dve.wait_ge(bank_full, paired(t - 2))
                src = gram[t % 2][:, :, 0:HALF * NV].rearrange("f k (c g) -> f g k c", g=NV)
                dve.transpose(grid[:, t % 2, 0:NV, :].rearrange("b g (k c) -> b g k c", k=2), src)\
                   .then_inc(grid_turned, 1)
                dve.wait_ge(grid_turned, t + 1)
                dve.tensor_copy(grid[:, t % 2, NV:NV + K, NV - K:NV],
                                grid[:, t % 2, 0:K, NV - K:NV]).then_inc(grid_ready, 1)
                dve.wait_ge(grid_ready, t + 1)
                one = grid[:, t % 2, 1, 0:1]
                diagonals = bass.AP(tensor=one.tensor, offset=one.offset,
                                    ap=[list(one.ap[0]), [QUAD + 1, NV], [QUAD, K]])
                dve.tensor_copy(packed[:, t % 2, :].rearrange("b (f k) -> b f k", k=K), diagonals)\
                   .then_inc(packed_ready, 1)

            def relu1(t):
                if t == 0:
                    dve.wait_ge(small_in, 64)
                dve.wait_ge(l1b, t + 1)
                if t >= 2:
                    dve.wait_ge(l2_done, t - 1)
                for c in (2, 3):
                    dve.tensor_scalar(h1[:, t % 2, c, :], topB[:, (c - 2) * P:(c - 1) * P], b1[:, c:c + 1], 0.0,
                                      ALU.add, ALU.max).then_inc(h1b_ready, 1)

            def copy_y(t):
                dve.wait_ge(l3_done, t + 1)
                dve.tensor_copy(y[0:1, t * P:(t + 1) * P], topB[0:1, 256:256 + P]).then_inc(y_ready, 1)

            for t in range(NT):
                if t >= 1:
                    copy_y(t - 1)
                make_grid(t)
                relu1(t)
            copy_y(NT - 1)

        @block.tensor
        def _(pe):
            filled = [0]

            def fill_bank(item):
                m = filled[0]
                filled[0] += 1
                if m >= 2:
                    pe.wait_ge(bank_copied, m - 1)
                dst = bank[m % 2]
                if item[0] == "lookup":
                    n = item[1]
                    for k in range(KT):
                        if k < KV:
                            pe.wait_ge(onehot_dve, n * KV + k + 1)
                        else:
                            pe.wait_ge(onehot_act, n * ACT_TILES + k - KV + 1)
                        if k == 0:
                            pe.wait_ge(high_ready, n + 1)
                        hot = onehot[:, (n % 2) * KT + k, :]
                        pe.matmul(dst[:, :], high[:, n % 2, k * D:(k + 1) * D], hot, start=(k == 0), stop=False)
                        if k == 0:
                            pe.wait_ge(low_ready, n + 1)
                        last = pe.matmul(dst[:, :], low[:, n % 2, k * D:(k + 1) * D], hot, start=False,
                                         stop=(k == KT - 1))
                elif item[0] == "pairs":
                    t = item[1]
                    pe.wait_ge(packed_ready, t + 1)
                    for k in range(NBLK):
                        last = pe.transpose(dst[0:PB, k * P:(k + 1) * P], packed[:, t % 2, k * PB:(k + 1) * PB],
                                            ident[:, :])
                else:
                    _, t, k = item
                    s, n = PER_BANK * k, min(PER_BANK, NG - PER_BANK * k)
                    pe.wait_ge(rows_in[t][k], 16 * n)
                    for x in range(n):
                        last = pe.transpose(dst[:, x * P:(x + 1) * P], rows[:, t, s + x, :], ident[:, :])
                last.then_inc(bank_full, 1)

            def make_gram(t):
                pe.wait_ge(bank_copied, vectors(t))
                if t == 0:
                    pe.wait_ge(dense_ready, 2)
                    pe.wait_ge(gram_zeroed, 2)
                if t >= 2:
                    pe.wait_ge(grid_turned, t - 1)
                for c in range(QUAD):
                    if c == HALF and t >= 1:
                        layer3(t - 1)
                    for i in range(4):
                        b = t * P + QUAD * i + c
                        col = (c % HALF) * NV
                        last = pe.matmul(gram[t % 2][QUAD * i:QUAD * i + NV, c // HALF, col:col + NV],
                                         vecs[:, b, 0:NV], vecs[:, b, 0:NV], start=True, stop=True)
                last.then_inc(gram_ready, 1)

            def chunk(c):
                return (topA, topB)[c // 2][:, (c % 2) * P:(c % 2 + 1) * P]

            def layer1_dense(t):
                if t >= 1:
                    pe.wait_ge(h2_ready, C2 * t)
                    pe.wait_ge(y_ready, t)
                for c in range(C1):
                    pe.matmul(chunk(c), wd[:, c * P:(c + 1) * P], dense[:, t * P:(t + 1) * P],
                              start=(c % 2 == 0), stop=False, skip_group_check=True)

            def layer1_pairs(t):
                if t == 0:
                    pe.wait_ge(wp_in, 16)
                pe.wait_ge(bank_copied, paired(t))
                for c in range(C1):
                    for k in range(NBLK):
                        last = pe.matmul(chunk(c), wp[:, k, c * P:(c + 1) * P], pairs[:, t % 2, k, :], start=False,
                                         stop=(k == NBLK - 1), skip_group_check=True)
                    if c == 1:
                        last.then_inc(l1a, 1)
                last.then_inc(l1b, 1)

            def layer2(t):
                pe.wait_ge(h1a_ready, 2 * (t + 1))
                for c in range(C1):
                    if c == 2:
                        pe.wait_ge(h1b_ready, 2 * (t + 1))
                    for c2 in range(C2):
                        last = pe.matmul(topA[:, 256 + c2 * P:256 + (c2 + 1) * P], w2[:, c, c2 * P:(c2 + 1) * P],
                                         h1[:, t % 2, c, :], start=(c == 0 and c2 == 0), stop=(c == C1 - 1),
                                         skip_group_check=True)
                last.then_inc(l2_done, 1)

            def layer3(t):
                pe.wait_ge(h2_ready, C2 * (t + 1))
                for c in range(C2):
                    last = pe.matmul(topB[0:1, 256:256 + P], w3[:, c:c + 1], h2[:, t % 2, c, :], start=(c == 0),
                                     stop=(c == C2 - 1))
                last.then_inc(l3_done, 1)

            pe.wait_ge(ident_ready, 1)
            for item in early:
                fill_bank(item)
            for t in range(NT):
                make_gram(t)
                if t == 0:
                    pe.wait_ge(small_in, 64)
                layer1_dense(t)
                for item in next_turns(t)[:2] + [("pairs", t)] + next_turns(t)[2:3]:
                    fill_bank(item)
                layer1_pairs(t)
                for item in next_turns(t)[3:]:
                    fill_bank(item)
                layer2(t)
            layer3(NT - 1)


def kernel(**inputs):
    import numpy as np
    import concourse.bacc as bacc
    from concourse.bass_utils import run_bass_kernel_spmd

    dense = np.asarray(inputs["r_dense_features"])
    ids = np.asarray(inputs["ids"])
    B, F = ids.shape
    tables = [np.ascontiguousarray(inputs[f"tbl_{f}"]) for f in range(F)]
    plan = Plan([t.shape[0] for t in tables])
    W_top1 = np.ascontiguousarray(inputs["W_top1"])
    C1, C2 = inputs["b_top1"].shape[0] // P, inputs["b_top2"].shape[0] // P

    order = [[plan.pair_row(f, (f + k) % plan.n) for f in range(plan.per_block * blk, plan.per_block * (blk + 1))
              for k in range(1, plan.steps + 1)] for blk in range(plan.blocks)]
    w_pairs = np.ascontiguousarray(np.stack([W_top1[rows] for rows in order], axis=1))

    by_tile = ids.reshape(B // P, P, F).transpose(1, 0, 2)
    arrays = {
        "dense_t": np.ascontiguousarray(dense.T),
        "gather_ids": np.ascontiguousarray(by_tile[:, :, plan.gathered]).reshape(P, -1),
        "product_ids": np.ascontiguousarray(ids.T[plan.by_product]),
        "w_pairs": w_pairs,
        "W_top1": W_top1,
        "W_top2": np.ascontiguousarray(inputs["W_top2"]),
        "b1_cols": np.ascontiguousarray(np.asarray(inputs["b_top1"]).reshape(C1, P).T),
        "b2_cols": np.ascontiguousarray(np.asarray(inputs["b_top2"]).reshape(C2, P).T),
        "w3_cols": np.ascontiguousarray(np.asarray(inputs["W_top3"]).reshape(C2, P).T),
    }
    arrays |= {f"tbl_{f}": t for f, t in enumerate(tables)}

    nc = bacc.Bacc("TRN2", target_bir_lowering=False, num_devices=1)
    ap = {n: nc.dram_tensor(n, a.shape, mybir.dt.from_np(a.dtype), kind="ExternalInput").ap()
          for n, a in arrays.items()}
    y = nc.dram_tensor("y_out", (B, 1), F32, kind="ExternalOutput").ap()
    build_tower(nc, plan, ap["dense_t"], ap["gather_ids"], ap["product_ids"],
                [ap[f"tbl_{f}"] for f in range(F)], ap["w_pairs"], ap["W_top1"], ap["W_top2"],
                ap["b1_cols"], ap["b2_cols"], ap["w3_cols"], y.rearrange("b o -> o b"))
    r = run_bass_kernel_spmd(nc, [arrays], core_ids=[0])
    return r.results[0]["y_out"]
```

```python
from contextlib import ExitStack

import concourse.bass as bass
from concourse import mybir
from concourse.alu_op_type import AluOpType as ALU

F32 = mybir.dt.float32
F32R = mybir.dt.float32r
I32 = mybir.dt.int32
ACT = mybir.ActivationFunctionType

P = 128
QUAD = 32
RING = 3
FIRST_COMPARES = 3
WARM_UP = 16
EXTRA_TURNS = 2
TURNS = ((1, 2, 2), (0, 1, 2))
ACT_TILES = 1


class Plan:

    EARLY = 8
    LATE = ((2, 0), (2, 1))
    ROWS = 1000

    def __init__(self, table_rows, tiles):
        small = [f for f, rows in enumerate(table_rows) if rows == self.ROWS]
        self.by_product = small[:self.EARLY + len(self.LATE)]
        self.first = [0] * self.EARLY + [first for first, _ in self.LATE]
        assert len(self.by_product) == len(self.first)
        assert [p for _, p in self.LATE] == sorted(p for _, p in self.LATE)
        always = [f for f in range(len(table_rows)) if f not in self.by_product]
        n_by_first = sorted(range(len(self.first)), key=lambda n: -self.first[n])
        tables = always + [self.by_product[n] for n in n_by_first]
        self.slots = [0] + [1 + f for f in tables]
        self.slot = [1 + tables.index(f) for f in self.by_product]
        self.gathered = [tables[:len(always) + sum(first > t for first in self.first)] for t in range(tiles)]
        self.n = len(self.slots)
        self.steps = (self.n - 1) // 2
        assert self.n % 2 == 1
        self.per_block = next(f for f in range(self.n, 0, -1) if self.n % f == 0 and f * self.steps <= P)
        self.blocks = self.n // self.per_block

    def pair_row(self, f, g):
        a, b = sorted((self.slots[f], self.slots[g]))
        return P + a * self.n - a * (a + 1) // 2 + (b - a - 1)


def build_tower(nc, plan, dense_t, gather_ids, product_ids, tables, w_pairs, W_top1, W_top2,
                b1_cols, b2_cols, w3_cols, out):
    D, B = dense_t.shape
    N1, N2 = W_top2.shape
    NT = B // P
    NE, NP = plan.EARLY, len(plan.by_product)
    NG = [len(tables_of_tile) for tables_of_tile in plan.gathered]
    row_at = [sum(NG[:t]) for t in range(NT + 1)]
    NV = plan.n
    K, FB, NBLK = plan.steps, plan.per_block, plan.blocks
    PB = FB * K
    KR = next(k for k in range(P, 0, -1) if plan.ROWS % k == 0)
    KT = plan.ROWS // KR
    KV = KT - ACT_TILES
    PER_BANK = 512 // P
    BANKS = 3
    cuts = [list(range(0, n, PER_BANK)) + [n] for n in NG]
    if cuts[-1][-1] - cuts[-1][-2] > 1:
        cuts[-1].insert(-1, NG[-1] - 1)
    NB = [len(c) - 1 for c in cuts]
    C1, C2 = N1 // P, N2 // P
    HALF = QUAD // 2
    assert ACT_TILES >= 1 and D == P and NV <= QUAD and KT * KR == plan.ROWS and HALF * NV <= 512 and C1 == 4
    assert C2 == 2 and NT >= 3 and plan.per_block - 1 + K < NV

    turns = [[("turn", t, k) for k in range(NB[t])] for t in range(NT)]
    early = []
    ahead = [item for tile in turns for item in tile][:NB[0] + EXTRA_TURNS]
    for n in range(NE):
        early.append(("lookup", n))
        if n >= 1 and ahead:
            early.append(ahead.pop(0))
    early += ahead
    late = [[NE + x for x, (_, phase) in enumerate(plan.LATE) if phase == t] for t in range(NT)]

    def steps(t):
        left = [item for item in turns[t + 1] if item not in early] if t + 1 < NT else []
        made = [("lookup", n) for n in late[t]]
        a, b, c = TURNS[min(t, 1)]
        return left[:a], [("pairs", t, 0)] + left[a:b] + [("pairs", t, 1)] + left[b:c], made + left[c:]

    order = list(early)
    for t in range(NT):
        for part in steps(t):
            order += part

    banks = [m % (BANKS + 3) if m < len(early) else m % BANKS for m in range(len(order))]
    emptied = [max([x for x in range(m) if banks[x] == banks[m]], default=-1) + 1 for m in range(len(order))]

    def looked_up(n):
        return order.index(("lookup", n)) + 1

    def pieces(n):
        return [range(0, KT // 2), range(KT // 2, KT)] if n == 0 else [range(KT)]

    def split(n):
        return sum(len(pieces(x)) for x in range(n + 1))

    def vectors(t):
        needed = [("turn", t, NB[t] - 1)] + [("lookup", n) for n in range(NP) if plan.first[n] <= t]
        return max(order.index(item) for item in needed) + 1

    def paired(t, part):
        return order.index(("pairs", t, part)) + 1

    parts = [range(0, 1), range(1, NBLK)]

    with ExitStack() as ctx:
        def sb(name, shape, dt=F32):
            return ctx.enter_context(nc.sbuf_tensor(name, shape, dt))

        def ps(name, shape):
            return ctx.enter_context(nc.psum_tensor(name, shape, F32))

        def sem(name):
            return ctx.enter_context(nc.semaphore(name))

        ids_g = sb("ids_g", [P, row_at[NT]], I32)
        ids_p = sb("ids_p", [KR, RING, B], I32)
        raw = sb("raw", [KR, RING, KT * D])
        high = sb("high", [KR, RING, KT * D], F32R)
        low = sb("low", [KR, RING, KT * D], F32R)
        onehot = sb("onehot", [KR, 2 * KT, B], F32R)
        row_int = sb("row_int", [P, KT], I32)
        row_no = sb("row_no", [P, KT])
        minus_row_no = sb("minus_row_no", [P, KT])
        distance = sb("distance", [KR, B])
        ident = sb("ident", [P, P])
        rows = sb("rows", [P, row_at[NT], D])
        dense = sb("dense", [D, B])
        vecs = sb("vecs", [D, B, NV])
        grid = sb("grid", [P, 2, NV + K, QUAD])
        packed = sb("packed", [P, 2, NBLK * PB])
        pairs = sb("pairs", [PB, 2, NBLK, P])
        wp = sb("wp", [PB, NBLK, N1])
        wd_ab = sb("wd_ab", [D, 2, N1])
        w2 = sb("w2", [P, C1, N2])
        w3 = sb("w3", [P, C2])
        b1 = sb("b1", [P, C1])
        b2 = sb("b2", [P, C2])
        h1 = sb("h1", [P, 2, C1, P])
        h2 = sb("h2", [P, 2, C2, P])
        y = sb("y", [1, B])

        turned = [ps(f"turned{k}", [P, 512]) for k in range(BANKS)]
        gram = ps("gram", [P, 2, 512])
        topA = ps("topA", [P, 512])
        topB = ps("topB", [P, 512])
        topC = ps("topC", [P, 512])
        bank = [(turned + [topA, topB, topC])[k] for k in banks]

        def layer2_out(t, c):
            return ([topC, turned[0]][c] if t == NT - 1 else topC)[:, c * P:(c + 1) * P]

        def layer3_out(t):
            return (topA if t == NT - 2 else topC)[0:1, C2 * P:(C2 + 1) * P]

        ids_g_in = sem("ids_g_in")
        table_in = [[sem(f"table_in{n}_{x}") for x in range(len(pieces(n)))] for n in range(NP)]
        ids_p_in = [sem(f"ids_p_in{n}") for n in range(NP)]
        dense_in = sem("dense_in")
        wp_in = sem("wp_in")
        wd_in = sem("wd_in")
        small_in = sem("small_in")
        rows_in = [[sem(f"rows_in{t}_{k}") for k in range(NB[t])] for t in range(NT)]
        out_done = sem("out_done")
        ident_zeroed = sem("ident_zeroed")
        gram_zeroed = sem("gram_zeroed")
        ident_ready = sem("ident_ready")
        iota_done = sem("iota_done")
        row_no_ready = sem("row_no_ready")
        high_ready = sem("high_ready")
        low_ready = sem("low_ready")
        onehot_dve = sem("onehot_dve")
        onehot_act = sem("onehot_act")
        distance_ready = sem("distance_ready")
        hot_used = sem("hot_used")
        bank_full = sem("bank_full")
        bank_copied = sem("bank_copied")
        dense_ready = sem("dense_ready")
        gram_ready = sem("gram_ready")
        grid_turned = sem("grid_turned")
        grid_ready = sem("grid_ready")
        packed_ready = sem("packed_ready")
        l1a = sem("l1a")
        l1b = sem("l1b")
        h1a_ready = sem("h1a_ready")
        h1b_ready = sem("h1b_ready")
        l2_done = sem("l2_done")
        h2_ready = sem("h2_ready")
        l3_done = sem("l3_done")
        y_ready = sem("y_ready")

        block = ctx.enter_context(nc.Block())

        @block.sync
        def _(sp):
            def table(n):
                if n >= RING:
                    sp.wait_ge(low_ready, split(n - RING))
                    sp.wait_ge(onehot_dve, (n - RING + 1) * KV)
                    sp.wait_ge(onehot_act, (n - RING + 1) * ACT_TILES)
                sp.dma_start(ids_p[:, n % RING, :],
                             product_ids[n:n + 1, :].to_broadcast([KR, B])).then_inc(ids_p_in[n], 16)
                rows_of = tables[plan.by_product[n]].rearrange("(p k) d -> p k d", k=KT)
                for x, ks in enumerate(pieces(n)):
                    sp.dma_start(raw[:, n % RING, ks.start * D:ks.stop * D].rearrange("p (k d) -> p k d", d=D),
                                 rows_of[:, ks.start:ks.stop, :]).then_inc(table_in[n][x], 16)

            def load_weights():
                sp.dma_start(wp[:, :, :], w_pairs).then_inc(wp_in, 16)
                sp.dma_start(w2[:, :, :], W_top2.rearrange("(c p) n -> p c n", p=P)).then_inc(small_in, 16)
                sp.dma_start(w3[:, :], w3_cols).then_inc(small_in, 16)
                sp.dma_start(b1[:, :], b1_cols).then_inc(small_in, 16)
                sp.dma_start(b2[:, :], b2_cols).then_inc(small_in, 16)

            sp.dma_start(ids_g[:, :], gather_ids).then_inc(ids_g_in, 16)
            for n in range(NE):
                table(n)
            sp.dma_start(dense[:, :], dense_t).then_inc(dense_in, 16)
            sp.dma_start(wd_ab[:, 0, :], W_top1[0:D, :]).then_inc(wd_in, 16)
            sp.dma_start(wd_ab[:, 1, :], W_top1[W_top1.shape[0] - D:, :]).then_inc(wd_in, 16)
            load_weights()
            for n in range(NE, NP):
                table(n)
            sp.wait_ge(y_ready, NT)
            sp.dma_start(out, y[:, :]).then_inc(out_done, 16)
            sp.wait_ge(out_done, 16)

        @block.gpsimd
        def _(pool):
            pool.iota(row_int[:, :], pattern=[[1, KT]], base=0, channel_multiplier=KT).then_inc(iota_done, 1)
            pool.memset(ident[:, :], 0.0).then_inc(ident_zeroed, 1)
            pool.wait_ge(ident_zeroed, 1)
            pool.affine_select(out=ident[:, :], in_=ident[:, :], compare_op=ALU.not_equal, fill=1.0, base=0,
                               pattern=[[-1, P]], channel_multiplier=1).then_inc(ident_ready, 1)
            pool.wait_ge(ids_g_in, 16)
            for t in range(NT):
                for k in range(NB[t]):
                    for s in range(cuts[t][k], cuts[t][k + 1]):
                        at = row_at[t] + s
                        pool.indirect_dma_start(
                            rows[:, at, :], None, tables[plan.gathered[t][s]],
                            bass.IndirectOffsetOnAxis(ap=ids_g[:, at:at + 1], axis=0),
                        ).then_inc(rows_in[t][k], 16)

        @block.scalar
        def _(act):
            def split_high(n):
                if n >= RING:
                    act.wait_ge(bank_full, looked_up(n - RING))
                for x, ks in enumerate(pieces(n)):
                    cols = slice(ks.start * D, ks.stop * D)
                    act.wait_ge(table_in[n][x], 16)
                    act.activation(high[:, n % RING, cols], raw[:, n % RING, cols], ACT.Copy).then_inc(high_ready, 1)

            def compare(n):
                first = P * plan.first[n]
                act.wait_ge(ids_p_in[n], 16)
                if n >= 2:
                    act.wait_ge(bank_full, looked_up(n - 2))
                for x in range(ACT_TILES):
                    made = n * ACT_TILES + x
                    k = KV + x
                    if made:
                        act.wait_ge(onehot_act, made)
                    act.activation(distance[:, first:B], ids_p[:, n % RING, first:B], ACT.Abs,
                                   bias=minus_row_no[0:KR, k:k + 1]).then_inc(distance_ready, 1)
                    act.wait_ge(distance_ready, made + 1)
                    act.activation(onehot[:, (n % 2) * KT + k, first:B], distance[:, first:B], ACT.Relu,
                                   bias=1.0, scale=-1.0).then_inc(onehot_act, 1)

            copied = [0]

            def copy_bank(item):
                m = copied[0]
                copied[0] += 1
                act.wait_ge(bank_full, m + 1)
                if item[0] == "lookup":
                    first = P * plan.first[item[1]]
                    dst, src = vecs[:, first:B, plan.slot[item[1]]], bank[m][:, first:B]
                elif item[0] == "pairs":
                    _, t, part = item
                    ks = parts[part]
                    if t >= 2 and part == 0:
                        act.wait_ge(l1b, t - 1)
                    dst = pairs[:, t % 2, ks.start:ks.stop, :]
                    src = bank[m][0:PB, 0:len(ks) * P].rearrange("p (k b) -> p k b", b=P)
                else:
                    _, t, k = item
                    s, n = cuts[t][k], cuts[t][k + 1] - cuts[t][k]
                    dst = vecs[:, t * P:(t + 1) * P, 1 + s:1 + s + n].rearrange("d b s -> d s b")
                    src = bank[m][:, 0:n * P].rearrange("d (s b) -> d s b", s=n)
                act.activation(dst, src, ACT.Copy).then_inc(bank_copied, 1)

            def relu1(t):
                if t == 0:
                    act.wait_ge(small_in, 64)
                act.wait_ge(l1a, t + 1)
                if t >= 2:
                    act.wait_ge(l2_done, C2 * (t - 1))
                for c in (0, 1):
                    act.activation(h1[:, t % 2, c, :], topA[:, c * P:(c + 1) * P], ACT.Relu,
                                   bias=b1[:, c:c + 1]).then_inc(h1a_ready, 1)

            def relu2(t):
                if t >= 2:
                    act.wait_ge(l3_done, t - 1)
                for c in range(C2):
                    act.wait_ge(l2_done, C2 * t + c + 1 if t == NT - 1 else C2 * (t + 1))
                    act.activation(h2[:, t % 2, c, :], layer2_out(t, c), ACT.Relu,
                                   bias=b2[:, c:c + 1]).then_inc(h2_ready, 1)

            split_high(0)
            act.wait_ge(row_no_ready, 2)
            compare(0)
            split_high(1)
            compare(1)
            for item in early:
                copy_bank(item)
                if item[0] == "lookup" and item[1] + 2 < NE:
                    split_high(item[1] + 2)
                    compare(item[1] + 2)
            for n in late[0]:
                split_high(n)
                compare(n)
            for t in range(NT):
                before_pairs, before_layer1, after = steps(t)
                for item in before_pairs + before_layer1:
                    copy_bank(item)
                if t >= 1:
                    relu2(t - 1)
                relu1(t)
                for n in late[t + 1] if t + 1 < NT else []:
                    split_high(n)
                    compare(n)
                for item in after:
                    copy_bank(item)
            relu2(NT - 1)

        @block.vector
        def _(dve):
            dve.memset(gram[:, :, :], 0.0).then_inc(gram_zeroed, 1)
            dve.wait_ge(iota_done, 1)
            dve.tensor_copy(row_no[:, :], row_int[:, :]).then_inc(row_no_ready, 1)
            dve.wait_ge(row_no_ready, 1)
            dve.tensor_scalar(minus_row_no[:, :], row_no[:, :], -1.0, None, ALU.mult).then_inc(row_no_ready, 1)

            def compare(n, k):
                if n >= 2:
                    dve.wait_ge(hot_used, (n - 2) * KV + k + 1)
                first = P * plan.first[n]
                dve.tensor_scalar(onehot[:, (n % 2) * KT + k, first:B], ids_p[:, n % RING, first:B],
                                  row_no[0:KR, k:k + 1], None, ALU.is_equal).then_inc(onehot_dve, 1)

            def prepare(n):
                ahead = FIRST_COMPARES if n == 0 else 1
                dve.wait_ge(ids_p_in[n], 16)
                for k in range(ahead):
                    compare(n, k)
                if n >= RING:
                    dve.wait_ge(bank_full, looked_up(n - RING))
                done = split(n) - len(pieces(n))
                for x, ks in enumerate(pieces(n)):
                    cols = slice(ks.start * D, ks.stop * D)
                    dve.wait_ge(table_in[n][x], 16)
                    dve.wait_ge(high_ready, done + x + 1)
                    dve.tensor_tensor(low[:, n % RING, cols], raw[:, n % RING, cols],
                                      high[:, n % RING, cols].bitcast(F32), ALU.subtract).then_inc(low_ready, 1)
                    for k in range(max(ahead, ks.start), min(KV, ks.stop)):
                        compare(n, k)

            for n in range(NE):
                prepare(n)
            dve.wait_ge(dense_in, 16)
            dve.tensor_copy(vecs[:, :, 0], dense[:, :]).then_inc(dense_ready, 1)
            dve.wait_ge(wd_in, 32)
            dve.tensor_tensor(wd_ab[:, 0, :], wd_ab[:, 0, :], wd_ab[:, 1, :], ALU.add).then_inc(dense_ready, 1)

            def make_grid(t):
                dve.wait_ge(gram_ready, t + 1)
                if t >= 2:
                    dve.wait_ge(bank_full, paired(t - 2, 1))
                src = gram[:, :, 0:HALF * NV].rearrange("f k (c g) -> f g k c", g=NV)
                dve.transpose(grid[:, t % 2, 0:NV, :].rearrange("b g (k c) -> b g k c", k=2), src)\
                   .then_inc(grid_turned, 1)
                dve.wait_ge(grid_turned, t + 1)
                pack(t, 0)
                dve.tensor_copy(grid[:, t % 2, NV:NV + K, NV - K:NV],
                                grid[:, t % 2, 0:K, NV - K:NV]).then_inc(grid_ready, 1)
                dve.wait_ge(grid_ready, t + 1)
                pack(t, 1)

            def pack(t, part):
                first, n = FB * parts[part].start, FB * len(parts[part])
                one = grid[:, t % 2, first + 1, first:first + 1]
                diagonals = bass.AP(tensor=one.tensor, offset=one.offset,
                                    ap=[list(one.ap[0]), [QUAD + 1, n], [QUAD, K]])
                dve.tensor_copy(packed[:, t % 2, first * K:(first + n) * K].rearrange("b (f k) -> b f k", k=K),
                                diagonals).then_inc(packed_ready, 1)

            def relu1(t):
                if t == 0:
                    dve.wait_ge(small_in, 64)
                dve.wait_ge(l1b, t + 1)
                if t >= 2:
                    dve.wait_ge(l2_done, C2 * (t - 1))
                for c in (2, 3):
                    dve.tensor_scalar(h1[:, t % 2, c, :], topB[:, (c - 2) * P:(c - 1) * P], b1[:, c:c + 1], 0.0,
                                      ALU.add, ALU.max).then_inc(h1b_ready, 1)

            def copy_y(t):
                dve.wait_ge(l3_done, t + 1)
                dve.tensor_copy(y[0:1, t * P:(t + 1) * P], layer3_out(t)).then_inc(y_ready, 1)

            for n in late[0]:
                prepare(n)
            for t in range(NT):
                if t >= 2:
                    copy_y(t - 2)
                make_grid(t)
                relu1(t)
                for n in late[t + 1] if t + 1 < NT else []:
                    prepare(n)
            copy_y(NT - 2)
            copy_y(NT - 1)

        @block.tensor
        def _(pe):
            filled = [0]

            def fill_bank(item):
                m = filled[0]
                filled[0] += 1
                if emptied[m]:
                    pe.wait_ge(bank_copied, emptied[m])
                dst = bank[m]
                if item[0] == "lookup":
                    n = item[1]
                    cols = slice(P * plan.first[n], B)
                    for k in range(KT):
                        if k < KV:
                            pe.wait_ge(onehot_dve, n * KV + k + 1)
                        else:
                            pe.wait_ge(onehot_act, n * ACT_TILES + k - KV + 1)
                        starts = [ks.start for ks in pieces(n)]
                        done = split(n) - len(starts)
                        if k in starts:
                            pe.wait_ge(high_ready, done + starts.index(k) + 1)
                        hot = onehot[:, (n % 2) * KT + k, cols]
                        pe.matmul(dst[:, cols], high[:, n % RING, k * D:(k + 1) * D], hot, start=(k == 0), stop=False)
                        if k in starts:
                            pe.wait_ge(low_ready, done + starts.index(k) + 1)
                        last = pe.matmul(dst[:, cols], low[:, n % RING, k * D:(k + 1) * D], hot, start=False,
                                         stop=(k == KT - 1))
                        if k < KV:
                            last.then_inc(hot_used, 1)
                elif item[0] == "pairs":
                    _, t, part = item
                    pe.wait_ge(packed_ready, 2 * t + part + 1)
                    for x, k in enumerate(parts[part]):
                        last = pe.transpose(dst[0:PB, x * P:(x + 1) * P], packed[:, t % 2, k * PB:(k + 1) * PB],
                                            ident[:, :])
                else:
                    _, t, k = item
                    s, n = cuts[t][k], cuts[t][k + 1] - cuts[t][k]
                    pe.wait_ge(rows_in[t][k], 16 * n)
                    for x in range(n):
                        last = pe.transpose(dst[:, x * P:(x + 1) * P], rows[:, row_at[t] + s + x, :], ident[:, :])
                last.then_inc(bank_full, 1)

            def make_gram(t):
                pe.wait_ge(bank_copied, vectors(t))
                if t == 0:
                    pe.wait_ge(dense_ready, 1)
                    pe.wait_ge(gram_zeroed, 1)
                else:
                    pe.wait_ge(grid_turned, t)
                for c in range(QUAD):
                    if c == HALF and t >= 2:
                        layer3(t - 2)
                    for i in range(4):
                        b = t * P + QUAD * i + c
                        col = (c % HALF) * NV
                        last = pe.matmul(gram[QUAD * i:QUAD * i + NV, c // HALF, col:col + NV],
                                         vecs[:, b, 0:NV], vecs[:, b, 0:NV], start=True, stop=True)
                last.then_inc(gram_ready, 1)

            def chunk(c):
                return (topA, topB)[c // 2][:, (c % 2) * P:(c % 2 + 1) * P]

            def layer1_dense(t, half):
                if t == 0:
                    pe.wait_ge(bank_copied, len(early))
                    pe.wait_ge(dense_ready, 2)
                else:
                    pe.wait_ge((h1a_ready, h1b_ready)[half], 2 * t)
                for c in (2 * half, 2 * half + 1):
                    pe.matmul(chunk(c), wd_ab[:, 0, c * P:(c + 1) * P], dense[:, t * P:(t + 1) * P],
                              start=(c % 2 == 0), stop=False, skip_group_check=True)

            def layer1_pairs(t):
                if t == 0:
                    pe.wait_ge(wp_in, 16)
                pe.wait_ge(bank_copied, paired(t, 0))
                for c in range(C1):
                    pe.matmul(chunk(c), wp[:, 0, c * P:(c + 1) * P], pairs[:, t % 2, 0, :], start=False,
                              stop=False, skip_group_check=True)
                pe.wait_ge(bank_copied, paired(t, 1))
                for c in range(C1):
                    for k in parts[1]:
                        last = pe.matmul(chunk(c), wp[:, k, c * P:(c + 1) * P], pairs[:, t % 2, k, :], start=False,
                                         stop=(k == NBLK - 1), skip_group_check=True)
                    if c == 1:
                        last.then_inc(l1a, 1)
                last.then_inc(l1b, 1)

            def layer2(t):
                if t >= 1:
                    pe.wait_ge(h2_ready, C2 * t)
                    pe.wait_ge(y_ready, min(t, NT - 2))
                pe.wait_ge(h1a_ready, 2 * (t + 1))
                for cs in (range(0, 2), range(2, C1)):
                    if cs.start == 2:
                        pe.wait_ge(h1b_ready, 2 * (t + 1))
                    for c2 in range(C2):
                        for c in cs:
                            last = pe.matmul(layer2_out(t, c2), w2[:, c, c2 * P:(c2 + 1) * P], h1[:, t % 2, c, :],
                                             start=(c == 0 and (c2 == 0 or t == NT - 1)), stop=(c == C1 - 1),
                                             skip_group_check=True)
                        if cs.start == 2:
                            last.then_inc(l2_done, 1)

            def layer3(t):
                pe.wait_ge(h2_ready, C2 * (t + 1))
                for c in range(C2):
                    last = pe.matmul(layer3_out(t), w3[:, c:c + 1], h2[:, t % 2, c, :], start=(c == 0),
                                     stop=(c == C2 - 1))
                last.then_inc(l3_done, 1)

            pe.wait_ge(ident_ready, 1)
            for _ in range(WARM_UP):
                pe.matmul(topB[:, 0:P], ident[:, :], ident[:, :], start=True, stop=True)
            for item in early:
                fill_bank(item)
            for t in range(NT):
                make_gram(t)
                if t == 0:
                    pe.wait_ge(small_in, 64)
                before_pairs, before_layer1, after = steps(t)
                if t == 0:
                    layer1_dense(0, 0)
                    layer1_dense(0, 1)
                else:
                    layer2(t - 1)
                for item in before_pairs + before_layer1:
                    fill_bank(item)
                layer1_pairs(t)
                for item in after[:-1]:
                    fill_bank(item)
                if t + 1 < NT:
                    layer1_dense(t + 1, 0)
                    fill_bank(after[-1])
                    layer1_dense(t + 1, 1)
            layer2(NT - 1)
            layer3(NT - 2)
            layer3(NT - 1)


def kernel(**inputs):
    import numpy as np
    import concourse.bacc as bacc
    from concourse.bass_utils import run_bass_kernel_spmd

    dense = np.asarray(inputs["r_dense_features"])
    ids = np.asarray(inputs["ids"])
    B, F = ids.shape
    tables = [np.ascontiguousarray(inputs[f"tbl_{f}"]) for f in range(F)]
    plan = Plan([t.shape[0] for t in tables], B // P)
    W_top1 = np.ascontiguousarray(inputs["W_top1"])
    C1, C2 = inputs["b_top1"].shape[0] // P, inputs["b_top2"].shape[0] // P

    order = [[plan.pair_row(f, (f + k) % plan.n) for f in range(plan.per_block * blk, plan.per_block * (blk + 1))
              for k in range(1, plan.steps + 1)] for blk in range(plan.blocks)]
    w_pairs = np.ascontiguousarray(np.stack([W_top1[rows] for rows in order], axis=1))

    by_tile = ids.reshape(B // P, P, F)
    arrays = {
        "dense_t": np.ascontiguousarray(dense.T),
        "gather_ids": np.concatenate([by_tile[t][:, plan.gathered[t]] for t in range(B // P)], axis=1),
        "product_ids": np.ascontiguousarray(ids.T[plan.by_product]),
        "w_pairs": w_pairs,
        "W_top1": W_top1,
        "W_top2": np.ascontiguousarray(inputs["W_top2"]),
        "b1_cols": np.ascontiguousarray(np.asarray(inputs["b_top1"]).reshape(C1, P).T),
        "b2_cols": np.ascontiguousarray(np.asarray(inputs["b_top2"]).reshape(C2, P).T),
        "w3_cols": np.ascontiguousarray(np.asarray(inputs["W_top3"]).reshape(C2, P).T),
    }
    arrays |= {f"tbl_{f}": t for f, t in enumerate(tables)}

    nc = bacc.Bacc("TRN2", target_bir_lowering=False, num_devices=1)
    ap = {n: nc.dram_tensor(n, a.shape, mybir.dt.from_np(a.dtype), kind="ExternalInput").ap()
          for n, a in arrays.items()}
    y = nc.dram_tensor("y_out", (B, 1), F32, kind="ExternalOutput").ap()
    build_tower(nc, plan, ap["dense_t"], ap["gather_ids"], ap["product_ids"],
                [ap[f"tbl_{f}"] for f in range(F)], ap["w_pairs"], ap["W_top1"], ap["W_top2"],
                ap["b1_cols"], ap["b2_cols"], ap["w3_cols"], y.rearrange("b o -> o b"))
    r = run_bass_kernel_spmd(nc, [arrays], core_ids=[0])
    return r.results[0]["y_out"]
```
